# Optimizing a Trainium2 kernel written in Bass

```python
import numpy as np
import jax
import jax.numpy as jnp

def _softmax(x, axis=-1):
    return jax.nn.softmax(x, axis=axis)

def _gelu(x):
    return jax.nn.gelu(x, approximate=True)

def _silu(x):
    return jax.nn.silu(x)

def _sigmoid(x):
    return jax.nn.sigmoid(x)

def _layernorm(x, axis=-1, eps=1e-05):
    m = jnp.mean(x, axis=axis, keepdims=True)
    v = jnp.var(x, axis=axis, keepdims=True)
    return (x - m) / jnp.sqrt(v + eps)

def _scatter_add(tgt, idx, src, axis=0):
    return tgt.at[idx].add(src)

def _segment_sum(src, seg, n):
    return jax.ops.segment_sum(src, seg, n)
kernel_name = 'mk_gnn_resnorm_d2_gnn_r64_e8f4e1'

def setup_inputs(seed: int=0):
    np.random.seed(seed)
    _w = jnp.asarray

    def _rec_inputs():
        import jax
        import jax.numpy as jnp
        _gk = jax.random.key(seed)
        x = -0.0003713 + 1 * jax.random.normal(jax.random.fold_in(_gk, 1), (50000, 256), jnp.float32)
        src = jax.random.randint(jax.random.fold_in(_gk, 2), (12500,), 0, 50000, jnp.int32)
        dst = jax.random.randint(jax.random.fold_in(_gk, 3), (12500,), 0, 50000, jnp.int32)
        _o = jnp.argsort(dst, stable=True)
        src = src[_o]
        dst = dst[_o]
        edge_attr_65 = 0.000166551 + 1.00014 * jax.random.normal(jax.random.fold_in(_gk, 11), (12500, 65), jnp.float32)
        return (x, src, dst, edge_attr_65)
    x, src, dst, edge_attr_65 = _rec_inputs()

    def _L0_gnn_setup():
        import jax, jax.numpy as jnp
        import numpy as np
        N = 50000
        E = 12500
        IN, HID, OUT = (256, 512, 256)
        key = jax.random.key(seed)
        ks = jax.random.split(key, 8)
        x = jax.random.normal(ks[0], (N, IN), dtype=jnp.float32)
        edge_index = jax.random.randint(ks[1], (2, E), 0, N, dtype=jnp.int64)

        def lin(k, fan_out, fan_in):
            s = 1.0 / np.sqrt(fan_in)
            return jax.random.uniform(k, (fan_out, fan_in), jnp.float32, -s, s)
        return {'x': x, 'edge_index': edge_index, 'W1l': lin(ks[2], HID, IN), 'b1': jnp.zeros((HID,), jnp.float32), 'W1r': lin(ks[3], HID, IN), 'W2l': lin(ks[4], OUT, HID), 'b2': jnp.zeros((OUT,), jnp.float32), 'W2r': lin(ks[5], OUT, HID)}
    _L0_gnn_all = _L0_gnn_setup()
    _L0_gnn_in = {k: v for k, v in _L0_gnn_all.items() if k in ('W1l', 'b1', 'W1r', 'W2l', 'b2', 'W2r')}
    del _L0_gnn_all

    def _L1_gnn_setup():
        import jax, jax.numpy as jnp
        import numpy as np
        N_NODES = 50000
        N_EDGES = 12500
        D = 256
        F_EDGE = 64
        LN_EPS = 1e-05
        key = jax.random.key(seed)
        ks = jax.random.split(key, 12)
        s = 0.05
        return {'x': jax.random.normal(ks[0], (N_NODES, D), jnp.float32), 'edge_index': jax.random.randint(ks[1], (2, N_EDGES), 0, N_NODES, jnp.int64), 'edge_attr': jax.random.normal(ks[2], (N_EDGES, F_EDGE + 1), jnp.float32), 'W_e1': jax.random.normal(ks[3], (D, F_EDGE), jnp.float32) * s, 'b_e1': jnp.zeros((D,), jnp.float32), 'W_e2': jax.random.normal(ks[4], (D, D), jnp.float32) * s, 'b_e2': jnp.zeros((D,), jnp.float32), 'W_le': jax.random.normal(ks[5], (D, D), jnp.float32) * s, 'b_le': jnp.zeros((D,), jnp.float32), 'W_g1': jax.random.normal(ks[6], (D, D), jnp.float32) * s, 'b_g1': jnp.zeros((D,), jnp.float32), 'ln_g': jnp.ones((D,), jnp.float32), 'ln_b': jnp.zeros((D,), jnp.float32), 'W_g2': jax.random.normal(ks[7], (D, D), jnp.float32) * s, 'b_g2': jnp.zeros((D,), jnp.float32)}
    _L1_gnn_all = _L1_gnn_setup()
    _L1_gnn_in = {k: v for k, v in _L1_gnn_all.items() if k in ('W_e1', 'b_e1', 'W_e2', 'b_e2', 'W_le', 'b_le', 'W_g1', 'b_g1', 'ln_g', 'ln_b', 'W_g2', 'b_g2')}
    del _L1_gnn_all
    return {'x': x, 'src': src, 'dst': dst, 'edge_attr_65': edge_attr_65, 'L0_gnn_W1l': _L0_gnn_in['W1l'], 'L0_gnn_b1': _L0_gnn_in['b1'], 'L0_gnn_W1r': _L0_gnn_in['W1r'], 'L0_gnn_W2l': _L0_gnn_in['W2l'], 'L0_gnn_b2': _L0_gnn_in['b2'], 'L0_gnn_W2r': _L0_gnn_in['W2r'], 'L1_gnn_W_e1': _L1_gnn_in['W_e1'], 'L1_gnn_b_e1': _L1_gnn_in['b_e1'], 'L1_gnn_W_e2': _L1_gnn_in['W_e2'], 'L1_gnn_b_e2': _L1_gnn_in['b_e2'], 'L1_gnn_W_le': _L1_gnn_in['W_le'], 'L1_gnn_b_le': _L1_gnn_in['b_le'], 'L1_gnn_W_g1': _L1_gnn_in['W_g1'], 'L1_gnn_b_g1': _L1_gnn_in['b_g1'], 'L1_gnn_ln_g': _L1_gnn_in['ln_g'], 'L1_gnn_ln_b': _L1_gnn_in['ln_b'], 'L1_gnn_W_g2': _L1_gnn_in['W_g2'], 'L1_gnn_b_g2': _L1_gnn_in['b_g2']}

def reference(x, src, dst, edge_attr_65, L0_gnn_W1l, L0_gnn_b1, L0_gnn_W1r, L0_gnn_W2l, L0_gnn_b2, L0_gnn_W2r, L1_gnn_W_e1, L1_gnn_b_e1, L1_gnn_W_e2, L1_gnn_b_e2, L1_gnn_W_le, L1_gnn_b_le, L1_gnn_W_g1, L1_gnn_b_g1, L1_gnn_ln_g, L1_gnn_ln_b, L1_gnn_W_g2, L1_gnn_b_g2):
    import jax
    import jax.numpy as jnp

    def _L0_gnn_ref(x, edge_index, W1l, b1, W1r, W2l, b2, W2r):
        import jax, jax.numpy as jnp
        import numpy as np
        N = 50000
        E = 12500
        IN, HID, OUT = (256, 512, 256)
        src, dst = (edge_index[0], edge_index[1])
        n = x.shape[0]
        deg = jax.ops.segment_sum(jnp.ones((src.shape[0],), x.dtype), dst, num_segments=n)
        inv_deg = 1.0 / jnp.maximum(deg, 1.0)

        def sage(h, Wl, b, Wr):
            agg = jax.ops.segment_sum(h[src], dst, num_segments=n) * inv_deg[:, None]
            return agg @ Wl.T + b + h @ Wr.T
        h = jax.nn.relu(sage(x, W1l, b1, W1r))
        z = sage(h, W2l, b2, W2r)
        return z

    def _L1_gnn_ref(x, edge_index, edge_attr, W_e1, b_e1, W_e2, b_e2, W_le, b_le, W_g1, b_g1, ln_g, ln_b, W_g2, b_g2):
        import jax, jax.numpy as jnp
        import numpy as np
        N_NODES = 50000
        N_EDGES = 12500
        D = 256
        F_EDGE = 64
        LN_EPS = 1e-05
        polarity = jnp.clip(edge_attr[:, 0:1], 0.0, 1.0)
        raw = edge_attr[:, 1:]
        e = jax.nn.relu(raw @ W_e1.T + b_e1) @ W_e2.T + b_e2
        gated = e * (polarity + 0.01)
        edge_emb = gated @ W_le.T + b_le
        src, dst = (edge_index[0], edge_index[1])
        msg = jax.nn.relu(x[src] + edge_emb)
        aggr = jax.ops.segment_sum(msg, dst, num_segments=x.shape[0])
        h = (x + aggr) @ W_g1.T + b_g1
        mu = jnp.mean(h, axis=-1, keepdims=True)
        var = jnp.mean(jnp.square(h - mu), axis=-1, keepdims=True)
        hn = (h - mu) * jax.lax.rsqrt(var + LN_EPS) * ln_g + ln_b
        return jax.nn.relu(hn) @ W_g2.T + b_g2
    edge_index = jnp.stack([src, dst])
    x = _layernorm(x + _L0_gnn_ref(x, edge_index, L0_gnn_W1l, L0_gnn_b1, L0_gnn_W1r, L0_gnn_W2l, L0_gnn_b2, L0_gnn_W2r), axis=-1)
    x = _layernorm(x + _L1_gnn_ref(x, edge_index, edge_attr_65, L1_gnn_W_e1, L1_gnn_b_e1, L1_gnn_W_e2, L1_gnn_b_e2, L1_gnn_W_le, L1_gnn_b_le, L1_gnn_W_g1, L1_gnn_b_g1, L1_gnn_ln_g, L1_gnn_ln_b, L1_gnn_W_g2, L1_gnn_b_g2), axis=-1)
    return x

_drawn_inputs = setup_inputs


def setup_inputs(seed=0):
    import zlib

    import numpy as np

    out = dict(_drawn_inputs(seed))
    spreads = {'L0_gnn_b1': (0.0, 0.1),
     'L0_gnn_b2': (0.0, 0.1),
     'L1_gnn_b_e1': (0.0, 2.0),
     'L1_gnn_b_e2': (0.0, 2.0),
     'L1_gnn_b_le': (0.0, 0.511),
     'L1_gnn_b_g1': (0.0, 0.1),
     'L1_gnn_ln_g': (1.0, 0.2),
     'L1_gnn_ln_b': (0.0, 0.1),
     'L1_gnn_b_g2': (0.0, 0.1)}
    factors = {'edge_attr_65': 4.509, 'L1_gnn_W_e1': 5.345, 'L1_gnn_W_e2': 4.24, 'L1_gnn_W_le': 4.056}
    for name, (base, spread) in spreads.items():
        noise = np.random.default_rng([zlib.crc32(name.encode()), seed]).standard_normal(out[name].shape)
        drawn = base * np.exp(spread * noise) if base else spread * noise
        out[name] = jnp.asarray(drawn.astype(out[name].dtype))
    for name, factor in factors.items():
        out[name] = (out[name] * factor).astype(out[name].dtype)
    return out
```

```python
import concourse.bass as bass
from concourse import mybir
from contextlib import ExitStack

F32 = mybir.dt.float32
F32R = mybir.dt.float32r
I32 = mybir.dt.int32
ALU = mybir.AluOpType
ACT = mybir.ActivationFunctionType

P = 128
D = 256
HID = 512
FE = 64
KD = D // P
KH = HID // P
N_NODES = 50000
N_EDGES = 12500
J = 4
GROUP = J * P
NG = -(-N_NODES // GROUP)
NPAD = NG * GROUP
NT = -(-N_EDGES // P)
EPAD = NT * P
NO_SLOT = EPAD
SKIP = 1 << 20
EPS = 1e-5
DEG = D
DW = D + 2


class Signals:

    def __init__(self, nc, ctx, prefix):
        self.nc, self.prefix, self.held = nc, prefix, []
        ctx.callback(self.clear)

    def sem(self, name):
        self.held.append(self.nc.alloc_semaphore(self.prefix + name))
        return self.held[-1]

    def clear(self):
        self.nc.clear_and_free_semaphores(self.held)
        self.nc.all_engine_barrier()


def fl(ap):
    return ap.bitcast(F32)


def pipelined(eng, n, stages):
    top = max(lag for _, lag in stages)
    head = 2 * (-(-(top + 2) // 2))
    tail = head + (n - head) // 2 * 2

    def peeled(steps):
        for i in steps:
            for stage, lag in stages:
                if 0 <= i - lag < n:
                    stage((i - lag) // 2, (i - lag) % 2)

    peeled(range(head))
    with eng.Fori(head // 2, tail // 2) as pair:
        for i in range(2):
            for stage, lag in stages:
                stage(pair + (i - lag) // 2, (i - lag) % 2)
    peeled(range(tail, n + top))


def first(k, u=0):
    return isinstance(k, int) and 2 * k + u == 0


def first_pair(k):
    return isinstance(k, int) and k == 0


def build_program(nc, A, out):
    ctx = ExitStack()
    with ctx:
        def dram(name, shape, dt=F32):
            return nc.dram_tensor(name, shape, dt, kind="Internal").ap()

        def sb(name, shape, dt=F32):
            return ctx.enter_context(nc.sbuf_tensor(name, shape, dt))

        x1_tab = dram("x1_tab", (NPAD, D))
        p1_tab = dram("p1_tab", (EPAD, HID))
        zd_tab = dram("zd_tab", (EPAD, D))
        x1d_tab = dram("x1d_tab", (EPAD, D))
        slot_tab = dram("slot_tab", (NPAD, 1), I32)

        WSHAPE = {"w1r": (P, KD, HID), "w1l": (P, KD, HID), "w2r": (P, KH, D), "w2l": (P, KH, D),
                  "wg1": (P, KD, D), "wg2": (P, KD, D), "wc": (P, KD, D), "we1": (FE + 1, 1, D)}
        W = {n: (sb(n + "_hi", s, F32R), sb(n + "_lo", s, F32R)) for n, s in WSHAPE.items()}
        B = {n: sb(n + "_row", (P, w)) for n, w in
             (("b1", HID), ("b2", D), ("bg1", D), ("bg2", D), ("ble", D), ("bc", D))}
        ln_g = sb("ln_g_col", (P, KD))
        ln_b = sb("ln_b_col", (P, KD))
        ident = sb("ident", (P, P))
        last_part = sb("last_part", (P, 1))
        minus_half = sb("minus_half", (P, J))
        idx_i = sb("idx_i", (P, NT, 4), I32)
        dst_f = sb("dst_f", (P, NT + 1))
        pol = sb("pol", (P, NT))
        inv_deg = sb("inv_deg", (P, NT))

        setup(nc, A, W, B, ln_g, ln_b, ident, last_part, minus_half, idx_i, dst_f, pol, slot_tab)
        dense(nc, A, W, B, ln_g, ln_b, ident, minus_half, x1_tab, out)
        edge0(nc, A, W, B, ident, last_part, idx_i, dst_f, inv_deg, slot_tab, p1_tab, zd_tab)
        edge1(nc, A, W, B, ident, last_part, minus_half, idx_i, dst_f, inv_deg, slot_tab,
              p1_tab, zd_tab, x1d_tab, x1_tab)
        edge2(nc, A, W, B, ln_g, ln_b, ident, last_part, minus_half, idx_i, dst_f, pol,
              x1d_tab, x1_tab, out)


def setup(nc, A, W, B, ln_g, ln_b, ident, last_part, minus_half, idx_i, dst_f, pol, slot_tab):
    ctx = ExitStack()
    with ctx:
        def sb(name, shape, dt=F32):
            return ctx.enter_context(nc.sbuf_tensor(name, shape, dt))

        sem = Signals(nc, ctx, "").sem

        raw = {n: sb(n + "_raw", W[n][0].shape) for n in W if n != "wc"}
        we2 = sb("we2_raw", (P, KD, D))
        wle = sb("wle_raw", (P, KD, D))
        be2 = sb("be2_col", (P, KD))
        be2_wide = sb("be2_wide", (P, KD, P))
        zeros = sb("zeros", (P, P))
        src_in = sb("src_in", (P, NT), I32)
        dst_in = sb("dst_in", (P, NT), I32)
        next_in = sb("next_in", (P, NT), I32)
        next_f = sb("next_f", (P, NT))
        same = sb("same", (P, NT))
        scat_f = sb("scat_f", (P, NT))
        pol_in = sb("pol_in", (P, NT))
        pol_c = sb("pol_c", (P, NT))
        no_slot = sb("no_slot", (P, NPAD // P), I32)
        ps_wc = ctx.enter_context(nc.psum_tensor("ps_wc", [P, KD * D], F32))
        ps_bc = ctx.enter_context(nc.psum_tensor("ps_bc", [P, D], F32))

        loads = sem("setup_loads")
        const = sem("setup_const")
        slot_const = sem("setup_slot_const")
        slot_out = sem("setup_slot_out")
        folded = sem("setup_folded")
        step = sem("setup_step")
        n_loads = [0]
        block = ctx.enter_context(nc.Block())

        pairs = [(raw["w1r"], A["w1r_t"]), (raw["w1l"], A["w1l_t"]), (raw["w2r"], A["w2r_t"]),
                 (raw["w2l"], A["w2l_t"]), (raw["wg1"], A["wg1_t"]), (raw["wg2"], A["wg2_t"]),
                 (wle, A["wle_t"]), (we2, A["we2"])]

        @block.sync
        def _(sp):
            def load(dst, src):
                sp.dma_start(dst, src).then_inc(loads, 16)
                n_loads[0] += 1

            for tile, src in pairs:
                load(tile[:], src.rearrange("(k p) n -> p k n", p=P))
            load(raw["we1"][0:FE, 0, :], A["we1_t"])
            load(raw["we1"][FE:FE + 1, 0, :], A["be1"].unsqueeze(0))
            for name in ("b1", "b2", "bg1", "bg2", "ble"):
                load(B[name][:], A[name].unsqueeze(0).to_broadcast((P, A[name].shape[0])))
            load(ln_g[:], A["ln_g"])
            load(ln_b[:], A["ln_b"])
            load(be2[:], A["be2"])
            load(src_in[:], A["src"])
            load(dst_in[:], A["dst"])
            load(next_in[:], A["dst_next"])
            load(pol_in[:], A["polarity"])
            sp.wait_ge(slot_const, 1)
            sp.dma_start(slot_tab.rearrange("(p m) o -> p (m o)", p=P), no_slot[:]).then_inc(slot_out, 16)
            sp.wait_ge(slot_out, 16)

        @block.gpsimd
        def _(pool):
            pool.memset(no_slot[:], NO_SLOT).then_inc(slot_const, 1)
            pool.memset(ident[:], 0.0).then_inc(const, 1)
            pool.memset(last_part[:], 0.0).then_inc(const, 1)
            pool.memset(minus_half[:], -0.5).then_inc(const, 1)
            pool.wait_ge(const, 3)
            pool.affine_select(out=ident[:], in_=ident[:], compare_op=ALU.not_equal, fill=1.0,
                               base=0, pattern=[[-1, P]], channel_multiplier=1).then_inc(const, 1)
            pool.affine_select(out=last_part[:], in_=last_part[:], compare_op=ALU.not_equal,
                               fill=1.0, base=1 - P, pattern=[[0, 1]],
                               channel_multiplier=1).then_inc(const, 1)
            pool.iota(idx_i[:, :, 3], pattern=[[P, NT]], base=0, channel_multiplier=1).then_inc(const, 1)

        @block.vector
        def _(dve):
            count = [0]

            def done(ins):
                count[0] += 1
                ins.then_inc(step, 1)
                dve.wait_ge(step, count[0])

            dve.memset(zeros[:], 0.0)
            done(dve.memset(dst_f[:, 0:1], -1.0))
            dve.wait_ge(loads, 16 * n_loads[0])
            for k in range(KD):
                done(dve.tensor_scalar(be2_wide[:, k, :], zeros[:], be2[:, k:k + 1], None, ALU.add))
            for name in raw:
                hi, lo = W[name]
                done(dve.tensor_copy(hi[:], raw[name][:]))
                done(dve.tensor_tensor(lo[:], raw[name][:], fl(hi[:]), ALU.subtract))
            done(dve.tensor_copy(idx_i[:, :, 0], src_in[:]))
            done(dve.tensor_copy(idx_i[:, :, 1], dst_in[:]))
            done(dve.tensor_copy(dst_f[:, 1:NT + 1], dst_in[:]))
            done(dve.tensor_copy(next_f[:], next_in[:]))
            done(dve.tensor_tensor(same[:], dst_f[:, 1:NT + 1], next_f[:], ALU.is_equal))
            done(dve.scalar_tensor_tensor(out=scat_f[:], in0=same[:], scalar=float(SKIP),
                                          in1=dst_f[:, 1:NT + 1], op0=ALU.mult, op1=ALU.add))
            done(dve.tensor_copy(idx_i[:, :, 2], scat_f[:]))
            done(dve.tensor_scalar(pol_c[:], pol_in[:], 0.0, 1.0, ALU.max, ALU.min))
            done(dve.tensor_scalar(pol[:], pol_c[:], 0.01, None, ALU.add))
            dve.wait_ge(folded, 1)
            hi, lo = W["wc"]
            ps = ps_wc[:].rearrange("p (k n) -> p k n", k=KD)
            done(dve.tensor_copy(hi[:], ps))
            done(dve.tensor_tensor(lo[:], ps, fl(hi[:]), ALU.subtract))
            done(dve.tensor_copy(B["bc"][:], ps_bc[:]))

        @block.tensor
        def _(pe):
            pe.wait_ge(loads, 16 * n_loads[0])
            pe.wait_ge(step, 1 + KD)
            for m in range(KD):
                for k in range(KD):
                    pe.matmul(ps_wc[:, m * D:(m + 1) * D], we2[:, k, m * P:(m + 1) * P], wle[:, k, :],
                              start=(k == 0), stop=(k == KD - 1))
            for k in range(KD):
                mm = pe.matmul(ps_bc[:], be2_wide[:, k, :], wle[:, k, :], start=(k == 0), stop=(k == KD - 1))
            mm.then_inc(folded, 1)


def product(pe, ps, left, right, n_k):
    for k in range(n_k):
        pe.matmul(ps, left(0, k), right(0, k), start=(k == 0), stop=False)
        pe.matmul(ps, left(0, k), right(1, k), start=False, stop=False)
    for k in range(n_k):
        last = pe.matmul(ps, left(1, k), right(0, k), start=False, stop=(k == n_k - 1))
    return last


def dense(nc, A, W, B, ln_g, ln_b, ident, minus_half, x1_tab, out):
    ctx = ExitStack()
    with ctx:
        def sb(name, shape, dt=F32):
            return ctx.enter_context(nc.sbuf_tensor("d_" + name, shape, dt))

        def two(name, shape, dt=F32):
            return [sb(f"{name}{u}", shape, dt) for u in range(2)]

        sem = Signals(nc, ctx, "d_").sem

        def ps(name, width=512):
            return ctx.enter_context(nc.psum_tensor("d_" + name, [P, width], F32))

        ROWS = [P, J, D]
        x = two("x", ROWS)
        xb = two("xb", ROWS)
        xT = [two("xT_hi", [P, KD, GROUP], F32R), two("xT_lo", [P, KD, GROUP], F32R)]
        hf = two("hf", [P, GROUP])
        hT = [two("hT_hi", [P, KH, GROUP], F32R), two("hT_lo", [P, KH, GROUP], F32R)]
        zs = sb("zs", ROWS)
        x1 = two("x1", ROWS)
        x1b = two("x1b", ROWS)
        x1T = [sb("x1T_hi", [P, KD, GROUP], F32R), sb("x1T_lo", [P, KD, GROUP], F32R)]
        us = sb("us", ROWS)
        hn = sb("hn", ROWS)
        hnf = sb("hnf", [P, KD, GROUP])
        hnT = [sb("hnT_hi", [P, KD, GROUP], F32R), sb("hnT_lo", [P, KD, GROUP], F32R)]
        os_ = sb("os", ROWS)
        y = two("y", ROWS)
        LN = {n: (sb(n + "_st", [P, J, 6]), sb(n + "_mv", [P, J, 2]), sb(n + "_ve", [P, J]),
                  sb(n + "_rs", [P, J])) for n in ("z", "u", "o")}
        b1_col = sb("b1_col", [P, KH])
        psT = ps("psT", 1024)
        psH = [ps("psH0"), ps("psH1")]
        psM = [ps("psM0", 1024), ps("psM1", 1024)]

        x_in = [sem("x_in0"), sem("x_in1")]
        y_out = [sem("y_out0"), sem("y_out1")]
        x1_out = [sem("x1_out0"), sem("x1_out1")]
        b1_in = sem("b1_in")
        xb_ok = sem("xb_ok")
        x1b_ok = sem("x1b_ok")
        xT_ps, xT_hi, xT_lo = sem("xT_ps"), sem("xT_hi"), sem("xT_lo")
        x1T_ps, x1T_hi, x1T_lo = sem("x1T_ps"), sem("x1T_hi"), sem("x1T_lo")
        hnT_ps, hnT_hi, hnT_lo = sem("hnT_ps"), sem("hnT_hi"), sem("hnT_lo")
        h_ps, h_hi, h_lo = sem("h_ps"), sem("h_hi"), sem("h_lo")
        M_ps = {n: sem(n + "_ps") for n in "zuo"}
        summed = {n: sem(n + "_sum") for n in "zuo"}
        moments = {n: sem(n + "_moments") for n in "zuo"}
        var_ok = {n: sem(n + "_var") for n in "zuo"}
        rstd = {n: sem(n + "_rstd") for n in "zuo"}
        normed = {n: sem(n + "_normed") for n in "zuo"}
        block = ctx.enter_context(nc.Block())

        x_v = A["x"].rearrange("(g p j) d -> g p (j d)", p=P, j=J)
        x1_v = x1_tab.rearrange("(g p j) d -> g p (j d)", p=P, j=J)
        y_v = out.rearrange("(g p j) d -> g p (j d)", p=P, j=J)

        def rows(tab, k, u):
            return tab[bass.ds(2 * k + u, 1), :, :].rearrange("g p n -> p (g n)")

        def flat(t):
            return t[:].rearrange("p j d -> p (j d)")

        @block.sync
        def _(sp):
            def load_x(k, u):
                if not first_pair(k):
                    sp.wait_ge(xT_ps, 2 * k + u - 1)
                    sp.wait_ge(xb_ok, 2 * k + u - 1)
                sp.dma_start(flat(x[u]), rows(x_v, k, u)).then_inc(x_in[u], 16)

            def store_x1(k, u):
                sp.wait_ge(normed["z"], 2 * k + u + 1)
                sp.dma_start(rows(x1_v, k, u), flat(x1[u])).then_inc(x1_out[u], 16)

            def store_y(k, u):
                sp.wait_ge(normed["o"], 2 * k + u + 1)
                sp.dma_start(rows(y_v, k, u), flat(y[u])).then_inc(y_out[u], 16)

            pipelined(sp, NG, [(load_x, 0), (store_x1, 3), (store_y, 5)])
            for u in range(2):
                n = 16 * len(range(u, NG, 2))
                sp.wait_ge(x1_out[u], n)
                sp.wait_ge(y_out[u], n)

        @block.tensor
        def _(pe):
            def turn(tile):
                for c in range(KD):
                    for j in range(J):
                        last = pe.transpose(psT[:, c * GROUP + j * P:c * GROUP + (j + 1) * P],
                                            tile[:, j, c * P:(c + 1) * P], ident[:])
                return last

            def turn_x(k, u):
                pe.wait_ge(x_in[u], 16 * (k + 1))
                if not first(k, u):
                    pe.wait_ge(xT_lo, 2 * k + u)
                    if not (isinstance(k, int) and 2 * k + u < 3):
                        pe.wait_ge(x1T_lo, 2 * k + u - 2)
                    if not (isinstance(k, int) and 2 * k + u < 4):
                        pe.wait_ge(hnT_hi, 2 * k + u - 3)
                turn(x[u]).then_inc(xT_ps, 1)

            def h(blocks):
                def stage(k, u):
                    pe.wait_ge(xT_hi, 2 * k + u + 1)
                    pe.wait_ge(xT_lo, 2 * k + u + 1)
                    for m in blocks:
                        if not (first(k, u) and m < 2):
                            pe.wait_ge(h_hi, 8 * k + 4 * u + m - 1)
                        product(pe, psH[m % 2][:], lambda s, c: W["w1r"][s][:, c, m * P:(m + 1) * P],
                                lambda s, c: xT[s][u][:, c, :], KD).then_inc(h_ps, 1)
                return stage

            def z(k, u):
                pe.wait_ge(h_hi, 8 * k + 4 * u + 4)
                pe.wait_ge(h_lo, 8 * k + 4 * u + 4)
                if not (isinstance(k, int) and 2 * k + u < 3):
                    pe.wait_ge(summed["o"], 4 * k + 2 * u - 4)
                for j in range(J):
                    last = product(pe, psM[u][:, j * D:(j + 1) * D],
                                   lambda s, c: hT[s][u][:, c, j * P:(j + 1) * P],
                                   lambda s, c: W["w2r"][s][:, c, :], KH)
                    if j & 1:
                        last.then_inc(M_ps["z"], 1)

            def turn_x1(k, u):
                pe.wait_ge(normed["z"], 2 * k + u + 1)
                if not first(k, u):
                    pe.wait_ge(hnT_hi, 2 * k + u)
                pe.wait_ge(xT_lo, 2 * k + u + 3 if not isinstance(k, int) else min(2 * k + u + 3, NG))
                turn(x1[u]).then_inc(x1T_ps, 1)

            def uu(k, u):
                pe.wait_ge(x1T_hi, 2 * k + u + 1)
                pe.wait_ge(x1T_lo, 2 * k + u + 1)
                pe.wait_ge(summed["z"], 4 * k + 2 * u + 4 if not isinstance(k, int) else 2 * min(2 * k + u + 2, NG))
                if not (isinstance(k, int) and 2 * k + u < 2):
                    pe.wait_ge(summed["o"], 4 * k + 2 * u - 2)
                for j in range(J):
                    last = product(pe, psM[1 - u][:, j * D:(j + 1) * D],
                                   lambda s, c: x1T[s][:, c, j * P:(j + 1) * P],
                                   lambda s, c: W["wg1"][s][:, c, :], KD)
                    if j & 1:
                        last.then_inc(M_ps["u"], 1)

            def turn_hn(k, u):
                pe.wait_ge(normed["u"], 2 * k + u + 1)
                pe.wait_ge(xT_lo, 2 * k + u + 4 if not isinstance(k, int) else min(2 * k + u + 4, NG))
                pe.wait_ge(x1T_lo, 2 * k + u + 1)
                turn(hn).then_inc(hnT_ps, 1)

            def o(k, u):
                pe.wait_ge(hnT_hi, 2 * k + u + 1)
                pe.wait_ge(hnT_lo, 2 * k + u + 1)
                pe.wait_ge(summed["u"], 4 * k + 2 * u + 2)
                for j in range(J):
                    last = product(pe, psM[1 - u][:, j * D:(j + 1) * D],
                                   lambda s, c: hnT[s][:, c, j * P:(j + 1) * P],
                                   lambda s, c: W["wg2"][s][:, c, :], KD)
                    if j & 1:
                        last.then_inc(M_ps["o"], 1)

            pipelined(pe, NG, [(z, 2), (turn_hn, 4), (h((0, 1)), 1), (turn_x1, 3), (h((2, 3)), 1), (o, 4),
                               (turn_x, 0), (uu, 3)])

        @block.scalar
        def _(act):
            def x_hi(k, u):
                act.wait_ge(xT_ps, 2 * k + u + 1)
                if not first_pair(k):
                    act.wait_ge(h_ps, 8 * k + 4 * u - 4)
                act.activation(xT[0][u][:], psT[:].rearrange("p (c n) -> p c n", c=KD),
                               ACT.Identity).then_inc(xT_hi, 1)

            def h_hi_(blocks):
                def stage(k, u):
                    for m in blocks:
                        act.wait_ge(h_ps, 8 * k + 4 * u + m + 1)
                        if not (first(k, u) and m < 2):
                            act.wait_ge(h_lo, 8 * k + 4 * u + m - 1)
                        if m == 0 and not first_pair(k):
                            act.wait_ge(M_ps["z"], 4 * k + 2 * u - 2)
                        bias = b1_col[:, m:m + 1]
                        act.activation(hf[m % 2][:], psH[m % 2][:], ACT.Relu, bias=bias)
                        act.activation(hT[0][u][:, m, :], psH[m % 2][:], ACT.Relu, bias=bias).then_inc(h_hi, 1)
                return stage

            def x1_hi(k, u):
                act.wait_ge(x1T_ps, 2 * k + u + 1)
                if not first(k, u):
                    act.wait_ge(M_ps["u"], 4 * k + 2 * u)
                act.activation(x1T[0][:], psT[:].rearrange("p (c n) -> p c n", c=KD),
                               ACT.Identity).then_inc(x1T_hi, 1)

            def hn_hi(k, u):
                act.wait_ge(hnT_ps, 2 * k + u + 1)
                if not first(k, u):
                    act.wait_ge(M_ps["o"], 4 * k + 2 * u)
                    act.wait_ge(hnT_lo, 2 * k + u)
                for c in range(KD):
                    sc = dict(bias=ln_b[:, c:c + 1], scale=ln_g[:, c:c + 1])
                    src = psT[:, c * GROUP:(c + 1) * GROUP]
                    act.activation(hnf[:, c, :], src, ACT.Relu, **sc)
                    last = act.activation(hnT[0][:, c, :], src, ACT.Relu, **sc)
                last.then_inc(hnT_hi, 1)

            act.dma_start(b1_col[:], A["b1_col"]).then_inc(b1_in, 16)
            act.wait_ge(b1_in, 16)
            pipelined(act, NG, [(hn_hi, 4), (h_hi_((0, 1)), 1), (x1_hi, 3), (h_hi_((2, 3)), 1), (x_hi, 0)])

        @block.vector
        def _(dve):
            def lo(name_hi, name_lo, tiles_hi, tiles_lo, before):
                def stage(k, u):
                    dve.wait_ge(name_hi, 2 * k + u + 1)
                    before(k, u)
                    dve.tensor_tensor(tiles_lo(u), psT[:].rearrange("p (c n) -> p c n", c=KD),
                                      fl(tiles_hi(u)), ALU.subtract).then_inc(name_lo, 1)
                return stage

            x_lo = lo(xT_hi, xT_lo, lambda u: xT[0][u][:], lambda u: xT[1][u][:], lambda k, u: None)
            x1_lo = lo(x1T_hi, x1T_lo, lambda u: x1T[0][:], lambda u: x1T[1][:], lambda k, u: None)

            def norm(n, bank, addend, total, result, before):
                st, mv, ve, rs = LN[n]

                def stage(k, u):
                    g1 = 2 * k + u + 1
                    if n == "z":
                        dve.wait_ge(xb_ok, g1)
                    if n == "o":
                        dve.wait_ge(x1b_ok, g1)
                    if not first(k, u):
                        dve.wait_ge(normed[n], 2 * k + u)
                    pm = psM[bank(u)][:].rearrange("p (j d) -> p j d", j=J)
                    for j in range(0, J, 2):
                        half = 4 * k + 2 * u + j // 2 + 1
                        dve.wait_ge(M_ps[n], half)
                        dve.tensor_tensor(total[:, j:j + 2, :], pm[:, j:j + 2, :], addend(u)[:, j:j + 2, :],
                                          ALU.add).then_inc(summed[n], 1)
                        dve.wait_ge(summed[n], half)
                        dve.bn_stats(st[:, j, :], total[:, j, :])
                        dve.bn_stats(st[:, j + 1, :], total[:, j + 1, :])
                    dve.drain()
                    for j in range(J):
                        last = dve.bn_aggr(mv[:, j, :], st[:, j, :])
                    last.then_inc(moments[n], 1)
                    dve.wait_ge(moments[n], g1)
                    dve.tensor_scalar(ve[:], mv[:, :, 1], EPS, None, ALU.add).then_inc(var_ok[n], 1)

                def scale(k, u):
                    dve.wait_ge(rstd[n], 2 * k + u + 1)
                    before(k, u)
                    for j in range(J):
                        last = dve.tensor_scalar(result(u)[:, j, :], total[:, j, :], mv[:, j, 0:1],
                                                 rs[:, j:j + 1], ALU.subtract, ALU.mult)
                    last.then_inc(normed[n], 1)
                return stage, scale

            def x1_free(k, u):
                if not first_pair(k):
                    dve.wait_ge(x1T_ps, 2 * k + u - 1)
                    dve.wait_ge(x1b_ok, 2 * k + u - 1)
                    dve.wait_ge(x1_out[u], 16 * k)

            def hn_free(k, u):
                if not first(k, u):
                    dve.wait_ge(hnT_ps, 2 * k + u)

            def y_free(k, u):
                if not first_pair(k):
                    dve.wait_ge(y_out[u], 16 * k)

            bg1 = B["bg1"][:].unsqueeze(1).to_broadcast((P, J, D))
            z1, z2 = norm("z", lambda u: u, lambda u: xb[u][:], zs, lambda u: x1[u], x1_free)
            u1, u2 = norm("u", lambda u: 1 - u, lambda u: bg1, us, lambda u: hn, hn_free)
            o1, o2 = norm("o", lambda u: 1 - u, lambda u: x1b[u][:], os_, lambda u: y[u], y_free)
            pipelined(dve, NG, [(u2, 4), (z1, 2), (x1_lo, 3), (z2, 2), (o1, 4), (x_lo, 0), (o2, 4),
                                (u1, 3)])

        @block.gpsimd
        def _(pool):
            b2 = B["b2"][:].unsqueeze(1).to_broadcast((P, J, D))
            bg2 = B["bg2"][:].unsqueeze(1).to_broadcast((P, J, D))

            def add_b2(k, u):
                pool.wait_ge(x_in[u], 16 * (k + 1))
                if not first_pair(k):
                    pool.wait_ge(summed["z"], 4 * k + 2 * u - 2)
                pool.tensor_tensor(xb[u][:], x[u][:], b2, ALU.add).then_inc(xb_ok, 1)

            def add_bg2(k, u):
                pool.wait_ge(normed["z"], 2 * k + u + 1)
                if not first_pair(k):
                    pool.wait_ge(summed["o"], 4 * k + 2 * u - 2)
                pool.tensor_tensor(x1b[u][:], x1[u][:], bg2, ALU.add).then_inc(x1b_ok, 1)

            def h_lo_(k, u):
                for m in range(KH):
                    pool.wait_ge(h_hi, 8 * k + 4 * u + m + 1)
                    pool.tensor_tensor(hT[1][u][:, m, :], hf[m % 2][:], fl(hT[0][u][:, m, :]),
                                       ALU.subtract).then_inc(h_lo, 1)

            def hn_lo(k, u):
                pool.wait_ge(hnT_hi, 2 * k + u + 1)
                pool.tensor_tensor(hnT[1][:], hnf[:], fl(hnT[0][:]), ALU.subtract).then_inc(hnT_lo, 1)

            def root(n):
                _, _, ve, rs = LN[n]

                def stage(k, u):
                    pool.wait_ge(var_ok[n], 2 * k + u + 1)
                    pool.tensor_tensor(rs[:], ve[:], minus_half[:, 0:J], ALU.pow).then_inc(rstd[n], 1)
                return stage

            pipelined(pool, NG, [(add_bg2, 3), (add_b2, 1), (root("z"), 2), (hn_lo, 4), (h_lo_, 1),
                                 (root("o"), 4), (root("u"), 3)])


def tile_pipeline(eng, stages):
    top = max(lag for _, lag in stages)
    head = 4 * (-(-(top + 4) // 4))
    tail = head + (NT - head) // 4 * 4

    def peeled(steps):
        for i in steps:
            for stage, lag in stages:
                if 0 <= i - lag < NT:
                    stage((i - lag) // 4, (i - lag) % 4)

    peeled(range(head))
    with eng.Fori(head // 4, tail // 4) as turn:
        for i in range(4):
            for stage, lag in stages:
                stage(turn + (i - lag) // 4, (i - lag) % 4)
    peeled(range(tail, NT + top))


def young(k, v, n):
    return isinstance(k, int) and 4 * k + v < n


def ready(eng, sem, k, v, back=0):
    if not young(k, v, back):
        eng.wait_ge(sem, 4 * k + v - back + 1)


def landed(eng, sems, k, v, back=0):
    if not young(k, v, back):
        eng.wait_ge(sems[(v - back) % 4], 16 * (k + (v - back) // 4 + 1))


def all_landed(eng, sems):
    for v in range(4):
        eng.wait_ge(sems[v], 16 * len(range(v, NT, 4)))


def edge_tools(nc, ctx, prefix):
    def sb(name, shape, dt=F32):
        return ctx.enter_context(nc.sbuf_tensor(prefix + name, shape, dt))

    def two(name, shape, dt=F32):
        return [sb(f"{name}{u}", shape, dt) for u in range(2)]

    def four(name, shape, dt=F32):
        return [sb(f"{name}{v}", shape, dt) for v in range(4)]

    sem = Signals(nc, ctx, prefix).sem

    def four_sems(name):
        return [sem(f"{name}{v}") for v in range(4)]

    def ps(name):
        return ctx.enter_context(nc.psum_tensor(prefix + name, [P, 512], F32))

    return sb, two, four, sem, four_sems, ps


def tile_rows(tab, k, v):
    return tab[bass.ds((4 * k + v) * P, P), :]


def column_of(table, k, v):
    return table[:, bass.ds(4 * k + v, 1), :].rearrange("p t n -> p (t n)")


def at(ap, column):
    return bass.IndirectOffsetOnAxis(ap=ap[:, column:column + 1], axis=0)


def flat(tile):
    return tile[:].rearrange("p c n -> p (c n)")


def edge0(nc, A, W, B, ident, last_part, idx_i, dst_f, inv_deg, slot_tab, p1_tab, zd_tab):
    ctx = ExitStack()
    with ctx:
        sb, two, four, sem, four_sems, ps = edge_tools(nc, ctx, "e0_")
        idx = four("idx", [P, 4], I32)
        dcol = four("dcol", [P, 2])
        dline = four("dline", [P, P], I32)
        xs = four("xs", [P, DW])
        xd = four("xd", [P, D])
        xdb = four("xdb", [P, D])
        xs_r = [two("xs_hi", [P, DW], F32R), two("xs_lo", [P, DW], F32R)]
        S = two("S", [P, P], F32R)
        R = two("R", [P, P], F32R)
        agg = [two("agg_hi", [P, DW], F32R), two("agg_lo", [P, DW], F32R)]
        inv = two("inv", [P, 1])
        mean = two("mean", [P, D])
        aT = [two("aT_hi", [P, 2 * KD, P], F32R), two("aT_lo", [P, 2 * KD, P], F32R)]
        p1 = two("p1", [P, HID])
        hs = two("hs", [P, HID])
        hd = two("hd", [P, HID])
        hT = [two("hT_hi", [P, KH, P], F32R), two("hT_lo", [P, KH, P], F32R)]
        zd = two("zd", [P, D])
        ps_agg = [ps("ps_agg0"), ps("ps_agg1")]
        ps_aT, ps_p, ps_q, ps_hT, ps_z = ps("ps_aT"), ps("ps_p"), ps("ps_q"), ps("ps_hT"), ps("ps_z")

        idx_ok = sem("idx_ok")
        dcol_ok = sem("dcol_ok")
        ones_ok = sem("ones_ok")
        waited = sem("waited")
        line_in = four_sems("line_in")
        xs_in = four_sems("xs_in")
        xd_in = four_sems("xd_in")
        slot_put = four_sems("slot_put")
        xs_hi, xs_lo, xdb_ok = sem("xs_hi"), sem("xs_lo"), sem("xdb_ok")
        S_ok, agg_ps, agg_hi, agg_lo = sem("S_ok"), sem("agg_ps"), sem("agg_hi"), sem("agg_lo")
        deg_ok, inv_ok, inv_kept, mean_ok = sem("deg_ok"), sem("inv_ok"), sem("inv_kept"), sem("mean_ok")
        aT_ps, aT_hi, aT_lo = sem("aT_ps"), sem("aT_hi"), sem("aT_lo")
        p_ps, q_ps, p1_ok, hs_ok, hd_ok = sem("p_ps"), sem("q_ps"), sem("p1_ok"), sem("hs_ok"), sem("hd_ok")
        hT_ps, hT_hi, hT_lo = sem("hT_ps"), sem("hT_hi"), sem("hT_lo")
        z_ps, zd_ok = sem("z_ps"), sem("zd_ok")
        p1_out = four_sems("p1_out")
        zd_out = four_sems("zd_out")
        block = ctx.enter_context(nc.Block())

        @block.sync
        def _(sp):
            def load_line(k, v):
                ready(sp, S_ok, k, v, 4)
                line = A["dst_line"][bass.ds((4 * k + v) * P, P)]
                sp.dma_start(dline[v][:], line.unsqueeze(0).to_broadcast((P, P))).then_inc(line_in[v], 16)

            def store_p1(k, v):
                ready(sp, p1_ok, k, v)
                sp.dma_start(tile_rows(p1_tab, k, v), p1[v % 2][:]).then_inc(p1_out[v], 16)

            def store_zd(k, v):
                ready(sp, zd_ok, k, v)
                sp.dma_start(tile_rows(zd_tab, k, v), zd[v % 2][:]).then_inc(zd_out[v], 16)

            tile_pipeline(sp, [(store_zd, 6), (store_p1, 4), (load_line, 0)])
            all_landed(sp, p1_out)
            all_landed(sp, zd_out)

        @block.gpsimd
        def _(pool):
            bound = pool.to_reg(NPAD - 1)
            pool.wait_ge(ones_ok, 1)

            def gathers(k, v):
                ready(pool, idx_ok, k, v)
                ready(pool, xs_lo, k, v, 4)
                pool.sem_inc(waited, 1)
                pool.indirect_dma_start(out=xs[v][:, 0:D], out_offset=None, in_=A["x"],
                                        in_offset=at(idx[v], 0),
                                        bounds_check=bound, oob_is_err=False).then_inc(xs_in[v], 16)
                ready(pool, aT_ps, k, v, 4)
                ready(pool, xdb_ok, k, v, 4)
                pool.sem_inc(waited, 1)
                pool.indirect_dma_start(out=xd[v][:], out_offset=None, in_=A["x"],
                                        in_offset=at(idx[v], 1),
                                        bounds_check=bound, oob_is_err=False).then_inc(xd_in[v], 16)
                pool.indirect_dma_start(out=slot_tab,
                                        out_offset=at(idx[v], 2),
                                        in_=idx[v][:, 3:4], in_offset=None,
                                        bounds_check=bound, oob_is_err=False).then_inc(slot_put[v], 16)

            def x_lo(k, v):
                ready(pool, xs_hi, k, v)
                ready(pool, agg_ps, k, v, 2)
                pool.tensor_tensor(xs_r[1][v % 2][:], xs[v][:], fl(xs_r[0][v % 2][:]), ALU.subtract).then_inc(xs_lo, 1)

            def x_b2(k, v):
                landed(pool, xd_in, k, v)
                ready(pool, zd_ok, k, v, 4)
                pool.tensor_tensor(xdb[v][:], xd[v][:], B["b2"][:], ALU.add).then_inc(xdb_ok, 1)

            tile_pipeline(pool, [(x_b2, 3), (x_lo, 1), (gathers, 0)])
            all_landed(pool, slot_put)

        @block.tensor
        def _(pe):
            def sums(k, v):
                ready(pe, S_ok, k, v)
                ready(pe, xs_hi, k, v)
                ready(pe, xs_lo, k, v)
                ready(pe, mean_ok, k, v, 2)
                ready(pe, agg_lo, k, v, 2)
                acc = ps_agg[v % 2][:, 0:DW]
                pe.matmul(acc, S[v % 2][:], xs_r[0][v % 2][:], start=True, stop=False)
                last = pe.matmul(acc, S[v % 2][:], xs_r[1][v % 2][:], start=False, stop=young(k, v, 1))
                if not young(k, v, 1):
                    ready(pe, agg_lo, k, v, 1)
                    pe.matmul(acc, R[v % 2][:], agg[0][(v + 1) % 2][:], start=False, stop=False)
                    last = pe.matmul(acc, R[v % 2][:], agg[1][(v + 1) % 2][:], start=False, stop=True)
                last.then_inc(agg_ps, 1)

            def turn_a(k, v):
                ready(pe, mean_ok, k, v)
                landed(pe, xd_in, k, v)
                ready(pe, aT_lo, k, v, 1)
                for c in range(KD):
                    pe.transpose(ps_aT[:, c * P:(c + 1) * P], mean[v % 2][:, c * P:(c + 1) * P], ident[:])
                for c in range(KD):
                    last = pe.transpose(ps_aT[:, (KD + c) * P:(KD + c + 1) * P], xd[v][:, c * P:(c + 1) * P],
                                        ident[:])
                last.then_inc(aT_ps, 1)

            def hidden(k, v):
                ready(pe, aT_hi, k, v)
                ready(pe, aT_lo, k, v)
                ready(pe, p1_ok, k, v, 1)
                product(pe, ps_p[:], lambda s, c: aT[s][v % 2][:, c, :], lambda s, c: W["w1l"][s][:, c, :],
                        KD).then_inc(p_ps, 1)
                ready(pe, hs_ok, k, v, 1)
                product(pe, ps_q[:], lambda s, c: aT[s][v % 2][:, KD + c, :], lambda s, c: W["w1r"][s][:, c, :],
                        KD).then_inc(q_ps, 1)

            def turn_h(k, v):
                ready(pe, hd_ok, k, v)
                ready(pe, hT_lo, k, v, 1)
                for c in range(KH):
                    last = pe.transpose(ps_hT[:, c * P:(c + 1) * P], hd[v % 2][:, c * P:(c + 1) * P], ident[:])
                last.then_inc(hT_ps, 1)

            def z(k, v):
                ready(pe, hT_hi, k, v)
                ready(pe, hT_lo, k, v)
                ready(pe, zd_ok, k, v, 1)
                product(pe, ps_z[:, 0:D], lambda s, c: hT[s][v % 2][:, c, :], lambda s, c: W["w2r"][s][:, c, :],
                        KH).then_inc(z_ps, 1)

            tile_pipeline(pe, [(z, 6), (turn_h, 5), (hidden, 4), (turn_a, 3), (sums, 2)])

        @block.scalar
        def _(act):
            def x_hi(k, v):
                landed(act, xs_in, k, v)
                ready(act, agg_ps, k, v, 2)
                act.activation(xs_r[0][v % 2][:], xs[v][:], ACT.Identity).then_inc(xs_hi, 1)

            def agg_hi_(k, v):
                ready(act, agg_ps, k, v)
                act.activation(agg[0][v % 2][:], ps_agg[v % 2][:, 0:DW], ACT.Identity).then_inc(agg_hi, 1)

            def a_hi(k, v):
                ready(act, aT_ps, k, v)
                ready(act, q_ps, k, v, 2)
                act.activation(flat(aT[0][v % 2]), ps_aT[:],
                               ACT.Identity).then_inc(aT_hi, 1)

            def relu(k, v):
                ready(act, hs_ok, k, v)
                ready(act, hT_ps, k, v, 2)
                act.activation(hd[v % 2][:], hs[v % 2][:], ACT.Relu).then_inc(hd_ok, 1)

            def h_hi(k, v):
                ready(act, hT_ps, k, v)
                ready(act, z_ps, k, v, 2)
                act.activation(flat(hT[0][v % 2]), ps_hT[:],
                               ACT.Identity).then_inc(hT_hi, 1)

            tile_pipeline(act, [(h_hi, 5), (relu, 4), (a_hi, 3), (agg_hi_, 2), (x_hi, 1)])

        @block.vector
        def _(dve):
            for u in range(4):
                dve.memset(xs[u][:, D:D + 1], 1.0)
                last = dve.memset(xs[u][:, D + 1:DW], 0.0)
            last.then_inc(ones_ok, 1)

            def columns(k, v):
                landed(dve, xs_in, k, v, 4)
                landed(dve, xd_in, k, v, 4)
                landed(dve, slot_put, k, v, 4)
                dve.tensor_copy(idx[v][:], column_of(idx_i, k, v)).then_inc(idx_ok, 1)
                ready(dve, S_ok, k, v, 4)
                dve.tensor_copy(dcol[v][:], dst_f[:, bass.ds(4 * k + v, 2)]).then_inc(dcol_ok, 1)

            def select(k, v):
                ready(dve, dcol_ok, k, v)
                landed(dve, line_in, k, v)
                ready(dve, agg_ps, k, v, 2)
                dve.tensor_scalar(R[v % 2][:], dline[v][:], dcol[v][:, 0:1], last_part[:], ALU.is_equal, ALU.mult)
                dve.tensor_scalar(S[v % 2][:], dline[v][:], dcol[v][:, 1:2], None, ALU.is_equal).then_inc(S_ok, 1)

            def agg_lo_(k, v):
                ready(dve, agg_hi, k, v)
                dve.tensor_tensor(agg[1][v % 2][:], ps_agg[v % 2][:, 0:DW], fl(agg[0][v % 2][:]),
                                  ALU.subtract).then_inc(agg_lo, 1)
                dve.reciprocal(inv[v % 2][:], ps_agg[v % 2][:, DEG:DEG + 1]).then_inc(inv_ok, 1)
                ready(dve, inv_ok, k, v)
                dve.tensor_copy(inv_deg[:, bass.ds(4 * k + v, 1)], inv[v % 2][:])
                ready(dve, aT_ps, k, v, 2)
                dve.tensor_scalar(mean[v % 2][:], ps_agg[v % 2][:, 0:D], inv[v % 2][:], None, ALU.mult).then_inc(mean_ok, 1)

            def a_lo(k, v):
                ready(dve, aT_hi, k, v)
                dve.tensor_tensor(flat(aT[1][v % 2]), ps_aT[:],
                                  fl(flat(aT[0][v % 2])), ALU.subtract).then_inc(aT_lo, 1)

            def add_p1(k, v):
                ready(dve, p_ps, k, v)
                landed(dve, p1_out, k, v, 2)
                dve.tensor_tensor(p1[v % 2][:], ps_p[:], B["b1"][:], ALU.add).then_inc(p1_ok, 1)
                ready(dve, p1_ok, k, v)
                ready(dve, q_ps, k, v)
                ready(dve, hd_ok, k, v, 2)
                dve.tensor_tensor(hs[v % 2][:], ps_q[:], p1[v % 2][:], ALU.add).then_inc(hs_ok, 1)

            def h_lo(k, v):
                ready(dve, hT_hi, k, v)
                dve.tensor_tensor(flat(hT[1][v % 2]), ps_hT[:],
                                  fl(flat(hT[0][v % 2])), ALU.subtract).then_inc(hT_lo, 1)

            def add_zd(k, v):
                ready(dve, z_ps, k, v)
                ready(dve, xdb_ok, k, v)
                landed(dve, zd_out, k, v, 2)
                dve.tensor_tensor(zd[v % 2][:], ps_z[:, 0:D], xdb[v][:], ALU.add).then_inc(zd_ok, 1)

            tile_pipeline(dve, [(add_zd, 6), (h_lo, 5), (add_p1, 4), (a_lo, 3), (agg_lo_, 2), (select, 1), (columns, 0)])


def edge1(nc, A, W, B, ident, last_part, minus_half, idx_i, dst_f, inv_deg, slot_tab,
          p1_tab, zd_tab, x1d_tab, x1_tab):
    ctx = ExitStack()
    with ctx:
        sb, two, four, sem, four_sems, ps = edge_tools(nc, ctx, "e1_")
        idx = four("idx", [P, 4], I32)
        put = four("put", [P, 1], I32)
        dcol = four("dcol", [P, 2])
        dline = four("dline", [P, P], I32)
        slot = four("slot", [P, 1], I32)
        xs = four("xs", [P, D])
        pg = four("pg", [P, HID])
        xT = [two("xT_hi", [P, KD, P], F32R), two("xT_lo", [P, KD, P], F32R)]
        hs = two("hs", [P, HID])
        hf = two("hf", [P, HID])
        h = [two("h_hi", [P, HID], F32R), two("h_lo", [P, HID], F32R)]
        S = two("S", [P, P], F32R)
        R = two("R", [P, P], F32R)
        agg = [two("agg_hi", [P, HID], F32R), two("agg_lo", [P, HID], F32R)]
        inv = two("inv", [P, 1])
        mean = two("mean", [P, HID])
        mT = [two("mT_hi", [P, KH, P], F32R), two("mT_lo", [P, KH, P], F32R)]
        zd = four("zd", [P, D])
        zs = two("zs", [P, D])
        st = two("st", [P, 6])
        mv = two("mv", [P, 2])
        ve = two("ve", [P, 1])
        rs = two("rs", [P, 1])
        x1d = four("x1d", [P, D])
        ps_xT, ps_mT, ps_z = ps("ps_xT"), ps("ps_mT"), ps("ps_z")
        ps_h = [ps("ps_h0"), ps("ps_h1")]
        ps_agg = [ps("ps_agg0"), ps("ps_agg1")]

        waited = sem("waited")
        idx_ok, dcol_ok, put_ok, pg_ok = sem("idx_ok"), sem("dcol_ok"), sem("put_ok"), sem("pg_ok")
        line_in, zd_in = four_sems("line_in"), four_sems("zd_in")
        slot_in, xs_in, pg_in = four_sems("slot_in"), four_sems("xs_in"), four_sems("pg_in")
        x1d_out, x1_out = four_sems("x1d_out"), four_sems("x1_out")
        xT_ps, xT_hi, xT_lo = sem("xT_ps"), sem("xT_hi"), sem("xT_lo")
        h_ps, hs_ok, h_hi, h_lo = sem("h_ps"), sem("hs_ok"), sem("h_hi"), sem("h_lo")
        S_ok, agg_ps, agg_hi, agg_lo = sem("S_ok"), sem("agg_ps"), sem("agg_hi"), sem("agg_lo")
        inv_ok, mean_ok = sem("inv_ok"), sem("mean_ok")
        mT_ps, mT_hi, mT_lo = sem("mT_ps"), sem("mT_hi"), sem("mT_lo")
        z_ps, zs_ok, mv_ok, ve_ok, rs_ok, x1d_ok = (sem(n) for n in (
            "z_ps", "zs_ok", "mv_ok", "ve_ok", "rs_ok", "x1d_ok"))
        block = ctx.enter_context(nc.Block())

        @block.sync
        def _(sp):
            def load_line(k, v):
                ready(sp, S_ok, k, v, 4)
                line = A["dst_line"][bass.ds((4 * k + v) * P, P)]
                sp.dma_start(dline[v][:], line.unsqueeze(0).to_broadcast((P, P))).then_inc(line_in[v], 16)

            def load_zd(k, v):
                ready(sp, zs_ok, k, v, 4)
                sp.dma_start(zd[v][:], tile_rows(zd_tab, k, v)).then_inc(zd_in[v], 16)

            def store_x1d(k, v):
                ready(sp, x1d_ok, k, v)
                sp.dma_start(tile_rows(x1d_tab, k, v), x1d[v][:]).then_inc(x1d_out[v], 16)

            tile_pipeline(sp, [(store_x1d, 7), (load_zd, 4), (load_line, 0)])
            all_landed(sp, x1d_out)

        @block.gpsimd
        def _(pool):
            node_bound = pool.to_reg(NPAD - 1)
            slot_bound = pool.to_reg(EPAD - 1)

            def gathers(k, v):
                ready(pool, idx_ok, k, v)
                landed(pool, pg_in, k, v, 4)
                pool.sem_inc(waited, 1)
                pool.indirect_dma_start(out=slot[v][:], out_offset=None, in_=slot_tab,
                                        in_offset=at(idx[v], 0), bounds_check=node_bound,
                                        oob_is_err=False).then_inc(slot_in[v], 16)
                ready(pool, xT_ps, k, v, 4)
                pool.sem_inc(waited, 1)
                pool.indirect_dma_start(out=xs[v][:], out_offset=None, in_=A["x"],
                                        in_offset=at(idx[v], 0), bounds_check=node_bound,
                                        oob_is_err=False).then_inc(xs_in[v], 16)

            def gather_p1(k, v):
                landed(pool, slot_in, k, v)
                ready(pool, pg_ok, k, v)
                pool.sem_inc(waited, 1)
                pool.indirect_dma_start(out=pg[v][:], out_offset=None, in_=p1_tab,
                                        in_offset=at(slot[v], 0), bounds_check=slot_bound,
                                        oob_is_err=False).then_inc(pg_in[v], 16)

            def h_lo_(k, v):
                ready(pool, h_hi, k, v)
                ready(pool, agg_ps, k, v, 2)
                pool.tensor_tensor(h[1][v % 2][:], hf[v % 2][:], fl(h[0][v % 2][:]),
                                   ALU.subtract).then_inc(h_lo, 1)

            def root(k, v):
                ready(pool, ve_ok, k, v)
                pool.tensor_tensor(rs[v % 2][:], ve[v % 2][:], minus_half[:, 0:1], ALU.pow).then_inc(rs_ok, 1)

            def scatter_x1(k, v):
                ready(pool, x1d_ok, k, v)
                ready(pool, put_ok, k, v)
                pool.sem_inc(waited, 1)
                pool.indirect_dma_start(out=x1_tab, out_offset=at(put[v], 0), in_=x1d[v][:], in_offset=None,
                                        bounds_check=node_bound, oob_is_err=False).then_inc(x1_out[v], 16)

            tile_pipeline(pool, [(scatter_x1, 7), (root, 6), (h_lo_, 3), (gather_p1, 1), (gathers, 0)])
            all_landed(pool, x1_out)

        @block.tensor
        def _(pe):
            def turn_x(k, v):
                landed(pe, xs_in, k, v)
                ready(pe, xT_lo, k, v, 1)
                for c in range(KD):
                    last = pe.transpose(ps_xT[:, c * P:(c + 1) * P], xs[v][:, c * P:(c + 1) * P], ident[:])
                last.then_inc(xT_ps, 1)

            def hidden(k, v):
                ready(pe, xT_hi, k, v)
                ready(pe, xT_lo, k, v)
                ready(pe, hs_ok, k, v, 2)
                product(pe, ps_h[v % 2][:], lambda s, c: xT[s][v % 2][:, c, :],
                        lambda s, c: W["w1r"][s][:, c, :], KD).then_inc(h_ps, 1)

            def sums(k, v):
                ready(pe, S_ok, k, v)
                ready(pe, h_hi, k, v)
                ready(pe, h_lo, k, v)
                ready(pe, mean_ok, k, v, 2)
                ready(pe, agg_lo, k, v, 2)
                acc = ps_agg[v % 2][:]
                pe.matmul(acc, S[v % 2][:], h[0][v % 2][:], start=True, stop=False)
                last = pe.matmul(acc, S[v % 2][:], h[1][v % 2][:], start=False, stop=young(k, v, 1))
                if not young(k, v, 1):
                    ready(pe, agg_lo, k, v, 1)
                    pe.matmul(acc, R[v % 2][:], agg[0][(v + 1) % 2][:], start=False, stop=False)
                    last = pe.matmul(acc, R[v % 2][:], agg[1][(v + 1) % 2][:], start=False, stop=True)
                last.then_inc(agg_ps, 1)

            def turn_mean(k, v):
                ready(pe, mean_ok, k, v)
                ready(pe, mT_lo, k, v, 1)
                for c in range(KH):
                    last = pe.transpose(ps_mT[:, c * P:(c + 1) * P], mean[v % 2][:, c * P:(c + 1) * P], ident[:])
                last.then_inc(mT_ps, 1)

            def z(k, v):
                ready(pe, mT_hi, k, v)
                ready(pe, mT_lo, k, v)
                ready(pe, zs_ok, k, v, 1)
                product(pe, ps_z[:, 0:D], lambda s, c: mT[s][v % 2][:, c, :],
                        lambda s, c: W["w2l"][s][:, c, :], KH).then_inc(z_ps, 1)

            tile_pipeline(pe, [(z, 6), (turn_mean, 5), (sums, 4), (hidden, 3), (turn_x, 2)])

        @block.scalar
        def _(act):
            def fill_b1(k, v):
                ready(act, hs_ok, k, v, 4)
                act.activation(pg[v][:], B["b1"][:], ACT.Identity).then_inc(pg_ok, 1)

            def x_hi(k, v):
                ready(act, xT_ps, k, v)
                ready(act, h_ps, k, v, 2)
                act.activation(flat(xT[0][v % 2]), ps_xT[:, 0:D], ACT.Identity).then_inc(xT_hi, 1)

            def relu(k, v):
                ready(act, hs_ok, k, v)
                ready(act, h_lo, k, v, 2)
                ready(act, agg_ps, k, v, 2)
                act.activation(hf[v % 2][:], hs[v % 2][:], ACT.Relu)
                act.activation(h[0][v % 2][:], hs[v % 2][:], ACT.Relu).then_inc(h_hi, 1)

            def agg_hi_(k, v):
                ready(act, agg_ps, k, v)
                act.activation(agg[0][v % 2][:], ps_agg[v % 2][:], ACT.Identity).then_inc(agg_hi, 1)

            def m_hi(k, v):
                ready(act, mT_ps, k, v)
                ready(act, z_ps, k, v, 2)
                act.activation(flat(mT[0][v % 2]), ps_mT[:], ACT.Identity).then_inc(mT_hi, 1)

            tile_pipeline(act, [(m_hi, 5), (agg_hi_, 4), (relu, 3), (x_hi, 2), (fill_b1, 0)])

        @block.vector
        def _(dve):
            def columns(k, v):
                landed(dve, slot_in, k, v, 4)
                landed(dve, xs_in, k, v, 4)
                dve.tensor_copy(idx[v][:], column_of(idx_i, k, v)).then_inc(idx_ok, 1)

            def x_lo(k, v):
                ready(dve, xT_hi, k, v)
                dve.tensor_tensor(flat(xT[1][v % 2]), ps_xT[:, 0:D], fl(flat(xT[0][v % 2])),
                                  ALU.subtract).then_inc(xT_lo, 1)

            def add_p1(k, v):
                ready(dve, h_ps, k, v)
                landed(dve, pg_in, k, v)
                ready(dve, h_hi, k, v, 2)
                dve.tensor_tensor(hs[v % 2][:], ps_h[v % 2][:], pg[v][:], ALU.add).then_inc(hs_ok, 1)

            def select(k, v):
                dve.tensor_copy(dcol[v][:], dst_f[:, bass.ds(4 * k + v, 2)]).then_inc(dcol_ok, 1)
                ready(dve, dcol_ok, k, v)
                landed(dve, line_in, k, v)
                ready(dve, agg_ps, k, v, 2)
                dve.tensor_scalar(R[v % 2][:], dline[v][:], dcol[v][:, 0:1], last_part[:],
                                  ALU.is_equal, ALU.mult)
                dve.tensor_scalar(S[v % 2][:], dline[v][:], dcol[v][:, 1:2], None, ALU.is_equal).then_inc(S_ok, 1)

            def agg_lo_(k, v):
                dve.tensor_copy(inv[v % 2][:], inv_deg[:, bass.ds(4 * k + v, 1)]).then_inc(inv_ok, 1)
                ready(dve, agg_hi, k, v)
                dve.tensor_tensor(agg[1][v % 2][:], ps_agg[v % 2][:], fl(agg[0][v % 2][:]),
                                  ALU.subtract).then_inc(agg_lo, 1)
                ready(dve, inv_ok, k, v)
                ready(dve, mT_ps, k, v, 2)
                dve.tensor_scalar(mean[v % 2][:], ps_agg[v % 2][:], inv[v % 2][:], None,
                                  ALU.mult).then_inc(mean_ok, 1)

            def m_lo(k, v):
                ready(dve, mT_hi, k, v)
                dve.tensor_tensor(flat(mT[1][v % 2]), ps_mT[:], fl(flat(mT[0][v % 2])),
                                  ALU.subtract).then_inc(mT_lo, 1)

            def add_z(k, v):
                ready(dve, z_ps, k, v)
                landed(dve, zd_in, k, v)
                dve.tensor_tensor(zs[v % 2][:], ps_z[:, 0:D], zd[v][:], ALU.add).then_inc(zs_ok, 1)
                variance(dve, zs[v % 2], st[v % 2], mv[v % 2], ve[v % 2], zs_ok, mv_ok, ve_ok, k, v)

            def norm(k, v):
                ready(dve, rs_ok, k, v)
                landed(dve, x1d_out, k, v, 4)
                landed(dve, x1_out, k, v, 4)
                dve.tensor_scalar(x1d[v][:], zs[v % 2][:], mv[v % 2][:, 0:1], rs[v % 2][:],
                                  ALU.subtract, ALU.mult).then_inc(x1d_ok, 1)
                dve.tensor_copy(put[v][:], idx_i[:, bass.ds(4 * k + v, 1), 2]).then_inc(put_ok, 1)

            tile_pipeline(dve, [(norm, 7), (add_z, 6), (m_lo, 5), (agg_lo_, 4), (add_p1, 3), (select, 3),
                                (x_lo, 2), (columns, 0)])


def variance(dve, total, st, mv, ve, total_ok, mv_ok, ve_ok, k, v):
    ready(dve, total_ok, k, v)
    dve.bn_stats(st[:], total[:])
    dve.drain()
    dve.bn_aggr(mv[:], st[:]).then_inc(mv_ok, 1)
    ready(dve, mv_ok, k, v)
    dve.tensor_scalar(ve[:], mv[:, 1:2], EPS, None, ALU.add).then_inc(ve_ok, 1)


def edge2(nc, A, W, B, ln_g, ln_b, ident, last_part, minus_half, idx_i, dst_f, pol,
          x1d_tab, x1_tab, out):
    ctx = ExitStack()
    with ctx:
        sb, two, four, sem, four_sems, ps = edge_tools(nc, ctx, "e2_")
        idx = four("idx", [P, 4], I32)
        put = four("put", [P, 1], I32)
        dcol = four("dcol", [P, 2])
        dline = four("dline", [P, P], I32)
        pcol = four("pcol", [P, 1])
        xg = four("xg", [P, D])
        raw = four("raw", [FE + 1, P])
        rw = [two("rw_hi", [FE + 1, P], F32R), two("rw_lo", [FE + 1, P], F32R)]
        rf = two("rf", [P, D])
        r = [two("r_hi", [P, KD, P], F32R), two("r_lo", [P, KD, P], F32R)]
        base = two("base", [P, D])
        part = two("part", [P, D])
        ms = two("ms", [P, D])
        mf = two("mf", [P, D])
        msg = [two("msg_hi", [P, D], F32R), two("msg_lo", [P, D], F32R)]
        S = two("S", [P, P], F32R)
        R = two("R", [P, P], F32R)
        agg = [two("agg_hi", [P, D], F32R), two("agg_lo", [P, D], F32R)]
        x1d = four("x1d", [P, D])
        x1b = four("x1b", [P, D])
        y = two("y", [P, D])
        yT = [two("yT_hi", [P, KD, P], F32R), two("yT_lo", [P, KD, P], F32R)]
        us = two("us", [P, D])
        hn = two("hn", [P, D])
        hf = two("hf", [P, KD, P])
        hT = [two("hT_hi", [P, KD, P], F32R), two("hT_lo", [P, KD, P], F32R)]
        os_ = two("os", [P, D])
        res = four("res", [P, D])
        st = {n: two("st" + n, [P, 6]) for n in "uo"}
        mv = {n: two("mv" + n, [P, 2]) for n in "uo"}
        ve = {n: two("ve" + n, [P, 1]) for n in "uo"}
        rs = {n: two("rs" + n, [P, 1]) for n in "uo"}
        ps_r, ps_e, ps_yT, ps_u, ps_hT, ps_o = (ps(n) for n in ("ps_r", "ps_e", "ps_yT", "ps_u", "ps_hT", "ps_o"))
        ps_agg = [ps("ps_agg0"), ps("ps_agg1")]

        waited = sem("waited")
        idx_ok, dcol_ok, put_ok, pcol_ok = sem("idx_ok"), sem("dcol_ok"), sem("put_ok"), sem("pcol_ok")
        line_in, raw_in, x1d_in = four_sems("line_in"), four_sems("raw_in"), four_sems("x1d_in")
        xg_in, out_put = four_sems("xg_in"), four_sems("out_put")
        rw_hi, rw_lo, r_ps, r_hi, r_lo = (sem(n) for n in ("rw_hi", "rw_lo", "r_ps", "r_hi", "r_lo"))
        e_ps, base_ok, part_ok, ms_ok = sem("e_ps"), sem("base_ok"), sem("part_ok"), sem("ms_ok")
        msg_hi, msg_lo, S_ok = sem("msg_hi"), sem("msg_lo"), sem("S_ok")
        agg_ps, agg_hi, agg_lo, y_ok = sem("agg_ps"), sem("agg_hi"), sem("agg_lo"), sem("y_ok")
        yT_ps, yT_hi, yT_lo = sem("yT_ps"), sem("yT_hi"), sem("yT_lo")
        u_ps, us_ok, hn_ok, x1b_ok = sem("u_ps"), sem("us_ok"), sem("hn_ok"), sem("x1b_ok")
        hT_ps, hT_hi, hT_lo = sem("hT_ps"), sem("hT_hi"), sem("hT_lo")
        o_ps, os_ok, res_ok = sem("o_ps"), sem("os_ok"), sem("res_ok")
        mv_ok = {n: sem("mv_ok" + n) for n in "uo"}
        ve_ok = {n: sem("ve_ok" + n) for n in "uo"}
        rs_ok = {n: sem("rs_ok" + n) for n in "uo"}
        block = ctx.enter_context(nc.Block())

        @block.sync
        def _(sp):
            def load_line(k, v):
                ready(sp, S_ok, k, v, 4)
                line = A["dst_line"][bass.ds((4 * k + v) * P, P)]
                sp.dma_start(dline[v][:], line.unsqueeze(0).to_broadcast((P, P))).then_inc(line_in[v], 16)

            def load_raw(k, v):
                ready(sp, rw_lo, k, v, 4)
                sp.dma_start(raw[v][:], A["edge_t"][:, bass.ds((4 * k + v) * P, P)]).then_inc(raw_in[v], 16)

            def load_x1d(k, v):
                ready(sp, y_ok, k, v, 4)
                ready(sp, x1b_ok, k, v, 4)
                sp.dma_start(x1d[v][:], tile_rows(x1d_tab, k, v)).then_inc(x1d_in[v], 16)

            tile_pipeline(sp, [(load_x1d, 3), (load_raw, 0), (load_line, 0)])

        @block.gpsimd
        def _(pool):
            node_bound = pool.to_reg(NPAD - 1)

            def gather_x1(k, v):
                ready(pool, idx_ok, k, v)
                ready(pool, ms_ok, k, v, 4)
                pool.sem_inc(waited, 1)
                pool.indirect_dma_start(out=xg[v][:], out_offset=None, in_=x1_tab,
                                        in_offset=at(idx[v], 0), bounds_check=node_bound,
                                        oob_is_err=False).then_inc(xg_in[v], 16)

            def r_lo_(k, v):
                ready(pool, r_hi, k, v)
                ready(pool, e_ps, k, v, 2)
                pool.tensor_tensor(flat(r[1][v % 2]), rf[v % 2][:], fl(flat(r[0][v % 2])),
                                   ALU.subtract).then_inc(r_lo, 1)

            def msg_lo_(k, v):
                ready(pool, msg_hi, k, v)
                ready(pool, agg_ps, k, v, 2)
                pool.tensor_tensor(msg[1][v % 2][:], mf[v % 2][:], fl(msg[0][v % 2][:]),
                                   ALU.subtract).then_inc(msg_lo, 1)

            def add_bg2(k, v):
                landed(pool, x1d_in, k, v)
                ready(pool, os_ok, k, v, 4)
                pool.tensor_tensor(x1b[v][:], x1d[v][:], B["bg2"][:], ALU.add).then_inc(x1b_ok, 1)

            def h_lo_(k, v):
                ready(pool, hT_hi, k, v)
                ready(pool, o_ps, k, v, 2)
                pool.tensor_tensor(flat(hT[1][v % 2]), flat(hf[v % 2]), fl(flat(hT[0][v % 2])),
                                   ALU.subtract).then_inc(hT_lo, 1)

            def root(n):
                def stage(k, v):
                    ready(pool, ve_ok[n], k, v)
                    pool.tensor_tensor(rs[n][v % 2][:], ve[n][v % 2][:], minus_half[:, 0:1],
                                       ALU.pow).then_inc(rs_ok[n], 1)
                return stage

            def scatter_out(k, v):
                ready(pool, res_ok, k, v)
                ready(pool, put_ok, k, v)
                pool.sem_inc(waited, 1)
                pool.indirect_dma_start(out=out, out_offset=at(put[v], 0), in_=res[v][:], in_offset=None,
                                        bounds_check=node_bound, oob_is_err=False).then_inc(out_put[v], 16)

            tile_pipeline(pool, [(scatter_out, 9), (root("o"), 8), (h_lo_, 7), (root("u"), 6), (add_bg2, 5),
                                 (msg_lo_, 3), (r_lo_, 2), (gather_x1, 0)])
            all_landed(pool, out_put)

        @block.tensor
        def _(pe):
            def mlp1(k, v):
                ready(pe, rw_hi, k, v)
                ready(pe, rw_lo, k, v)
                ready(pe, r_hi, k, v, 1)
                for c in range(KD):
                    last = product(pe, ps_r[:, c * P:(c + 1) * P],
                                   lambda s, _: W["we1"][s][:, 0, c * P:(c + 1) * P],
                                   lambda s, _: rw[s][v % 2][:], 1)
                last.then_inc(r_ps, 1)

            def mlp2(k, v):
                ready(pe, r_hi, k, v)
                ready(pe, r_lo, k, v)
                ready(pe, part_ok, k, v, 1)
                product(pe, ps_e[:, 0:D], lambda s, c: r[s][v % 2][:, c, :],
                        lambda s, c: W["wc"][s][:, c, :], KD).then_inc(e_ps, 1)

            def sums(k, v):
                ready(pe, S_ok, k, v)
                ready(pe, msg_hi, k, v)
                ready(pe, msg_lo, k, v)
                ready(pe, y_ok, k, v, 2)
                ready(pe, agg_lo, k, v, 2)
                acc = ps_agg[v % 2][:, 0:D]
                pe.matmul(acc, S[v % 2][:], msg[0][v % 2][:], start=True, stop=False)
                last = pe.matmul(acc, S[v % 2][:], msg[1][v % 2][:], start=False, stop=young(k, v, 1))
                if not young(k, v, 1):
                    ready(pe, agg_lo, k, v, 1)
                    pe.matmul(acc, R[v % 2][:], agg[0][(v + 1) % 2][:], start=False, stop=False)
                    last = pe.matmul(acc, R[v % 2][:], agg[1][(v + 1) % 2][:], start=False, stop=True)
                last.then_inc(agg_ps, 1)

            def turn(tile, target, given, taken, signal):
                def stage(k, v):
                    ready(pe, given, k, v)
                    ready(pe, taken, k, v, 1)
                    for c in range(KD):
                        last = pe.transpose(target[:, c * P:(c + 1) * P], tile[v % 2][:, c * P:(c + 1) * P],
                                            ident[:])
                    last.then_inc(signal, 1)
                return stage

            turn_y = turn(y, ps_yT, y_ok, yT_lo, yT_ps)
            turn_hn = turn(hn, ps_hT, hn_ok, hT_hi, hT_ps)

            def u(k, v):
                ready(pe, yT_hi, k, v)
                ready(pe, yT_lo, k, v)
                ready(pe, us_ok, k, v, 1)
                product(pe, ps_u[:, 0:D], lambda s, c: yT[s][v % 2][:, c, :],
                        lambda s, c: W["wg1"][s][:, c, :], KD).then_inc(u_ps, 1)

            def o(k, v):
                ready(pe, hT_hi, k, v)
                ready(pe, hT_lo, k, v)
                ready(pe, os_ok, k, v, 1)
                product(pe, ps_o[:, 0:D], lambda s, c: hT[s][v % 2][:, c, :],
                        lambda s, c: W["wg2"][s][:, c, :], KD).then_inc(o_ps, 1)

            tile_pipeline(pe, [(o, 8), (turn_hn, 7), (u, 6), (turn_y, 5), (sums, 4), (mlp2, 3), (mlp1, 2)])

        @block.scalar
        def _(act):
            def relu_r(k, v):
                ready(act, r_ps, k, v)
                ready(act, r_lo, k, v, 2)
                ready(act, e_ps, k, v, 2)
                act.activation(rf[v % 2][:], ps_r[:, 0:D], ACT.Relu)
                act.activation(flat(r[0][v % 2]), ps_r[:, 0:D], ACT.Relu).then_inc(r_hi, 1)

            def relu_msg(k, v):
                ready(act, ms_ok, k, v)
                ready(act, msg_lo, k, v, 2)
                ready(act, agg_ps, k, v, 2)
                act.activation(mf[v % 2][:], ms[v % 2][:], ACT.Relu)
                act.activation(msg[0][v % 2][:], ms[v % 2][:], ACT.Relu).then_inc(msg_hi, 1)

            def agg_hi_(k, v):
                ready(act, agg_ps, k, v)
                act.activation(agg[0][v % 2][:], ps_agg[v % 2][:, 0:D], ACT.Identity).then_inc(agg_hi, 1)

            def y_hi(k, v):
                ready(act, yT_ps, k, v)
                ready(act, u_ps, k, v, 2)
                act.activation(flat(yT[0][v % 2]), ps_yT[:, 0:D], ACT.Identity).then_inc(yT_hi, 1)

            def h_hi(k, v):
                ready(act, hT_ps, k, v)
                ready(act, hT_lo, k, v, 2)
                ready(act, o_ps, k, v, 2)
                for c in range(KD):
                    affine = dict(bias=ln_b[:, c:c + 1], scale=ln_g[:, c:c + 1])
                    act.activation(hf[v % 2][:, c, :], ps_hT[:, c * P:(c + 1) * P], ACT.Relu, **affine)
                    last = act.activation(hT[0][v % 2][:, c, :], ps_hT[:, c * P:(c + 1) * P], ACT.Relu, **affine)
                last.then_inc(hT_hi, 1)

            tile_pipeline(act, [(h_hi, 7), (y_hi, 5), (agg_hi_, 4), (relu_msg, 3), (relu_r, 2)])

        @block.vector
        def _(dve):
            def columns(k, v):
                landed(dve, xg_in, k, v, 4)
                dve.tensor_copy(idx[v][:], column_of(idx_i, k, v)).then_inc(idx_ok, 1)

            def split_raw(k, v):
                landed(dve, raw_in, k, v)
                ready(dve, r_ps, k, v, 2)
                dve.tensor_copy(rw[0][v % 2][:], raw[v][:]).then_inc(rw_hi, 1)
                ready(dve, rw_hi, k, v)
                dve.tensor_tensor(rw[1][v % 2][:], raw[v][:], fl(rw[0][v % 2][:]), ALU.subtract).then_inc(rw_lo, 1)

            def message(k, v):
                dve.tensor_copy(pcol[v][:], pol[:, bass.ds(4 * k + v, 1)]).then_inc(pcol_ok, 1)
                ready(dve, pcol_ok, k, v)
                dve.scalar_tensor_tensor(out=base[v % 2][:], in0=B["bc"][:], scalar=pcol[v][:], in1=B["ble"][:],
                                         op0=ALU.mult, op1=ALU.add).then_inc(base_ok, 1)
                ready(dve, base_ok, k, v)
                ready(dve, e_ps, k, v)
                dve.scalar_tensor_tensor(out=part[v % 2][:], in0=ps_e[:, 0:D], scalar=pcol[v][:],
                                         in1=base[v % 2][:], op0=ALU.mult, op1=ALU.add).then_inc(part_ok, 1)
                ready(dve, part_ok, k, v)
                landed(dve, xg_in, k, v)
                ready(dve, msg_hi, k, v, 2)
                dve.tensor_tensor(ms[v % 2][:], part[v % 2][:], xg[v][:], ALU.add).then_inc(ms_ok, 1)

            def select(k, v):
                dve.tensor_copy(dcol[v][:], dst_f[:, bass.ds(4 * k + v, 2)]).then_inc(dcol_ok, 1)
                ready(dve, dcol_ok, k, v)
                landed(dve, line_in, k, v)
                ready(dve, agg_ps, k, v, 2)
                dve.tensor_scalar(R[v % 2][:], dline[v][:], dcol[v][:, 0:1], last_part[:],
                                  ALU.is_equal, ALU.mult)
                dve.tensor_scalar(S[v % 2][:], dline[v][:], dcol[v][:, 1:2], None, ALU.is_equal).then_inc(S_ok, 1)

            def agg_lo_(k, v):
                ready(dve, agg_hi, k, v)
                dve.tensor_tensor(agg[1][v % 2][:], ps_agg[v % 2][:, 0:D], fl(agg[0][v % 2][:]),
                                  ALU.subtract).then_inc(agg_lo, 1)
                landed(dve, x1d_in, k, v)
                ready(dve, yT_ps, k, v, 2)
                dve.tensor_tensor(y[v % 2][:], ps_agg[v % 2][:, 0:D], x1d[v][:], ALU.add).then_inc(y_ok, 1)

            def y_lo(k, v):
                ready(dve, yT_hi, k, v)
                dve.tensor_tensor(flat(yT[1][v % 2]), ps_yT[:, 0:D], fl(flat(yT[0][v % 2])),
                                  ALU.subtract).then_inc(yT_lo, 1)

            def add_u(k, v):
                ready(dve, u_ps, k, v)
                dve.tensor_tensor(us[v % 2][:], ps_u[:, 0:D], B["bg1"][:], ALU.add).then_inc(us_ok, 1)
                variance(dve, us[v % 2], st["u"][v % 2], mv["u"][v % 2], ve["u"][v % 2],
                         us_ok, mv_ok["u"], ve_ok["u"], k, v)

            def norm_u(k, v):
                ready(dve, rs_ok["u"], k, v)
                ready(dve, hT_ps, k, v, 2)
                dve.tensor_scalar(hn[v % 2][:], us[v % 2][:], mv["u"][v % 2][:, 0:1], rs["u"][v % 2][:],
                                  ALU.subtract, ALU.mult).then_inc(hn_ok, 1)

            def add_o(k, v):
                ready(dve, o_ps, k, v)
                ready(dve, x1b_ok, k, v)
                dve.tensor_tensor(os_[v % 2][:], ps_o[:, 0:D], x1b[v][:], ALU.add).then_inc(os_ok, 1)
                variance(dve, os_[v % 2], st["o"][v % 2], mv["o"][v % 2], ve["o"][v % 2],
                         os_ok, mv_ok["o"], ve_ok["o"], k, v)

            def norm_o(k, v):
                ready(dve, rs_ok["o"], k, v)
                landed(dve, out_put, k, v, 4)
                dve.tensor_scalar(res[v][:], os_[v % 2][:], mv["o"][v % 2][:, 0:1], rs["o"][v % 2][:],
                                  ALU.subtract, ALU.mult).then_inc(res_ok, 1)
                dve.tensor_copy(put[v][:], idx_i[:, bass.ds(4 * k + v, 1), 2]).then_inc(put_ok, 1)

            tile_pipeline(dve, [(norm_o, 9), (add_o, 8), (norm_u, 7), (add_u, 6), (y_lo, 5), (agg_lo_, 4),
                                (message, 3), (select, 3), (split_raw, 1), (columns, 0)])


def kernel(**inputs):
    import numpy as np
    import concourse.bacc as bacc
    from concourse.bass_utils import run_bass_kernel_spmd

    a = {name.replace("L0_gnn_", "").replace("L1_gnn_", ""): np.asarray(v) for name, v in inputs.items()}

    def rows(v, n, fill=0):
        return np.concatenate([v, np.full((n - v.shape[0],) + v.shape[1:], fill, v.dtype)])

    def by_tile(v):
        return v.reshape(NT, P).T

    def column(v):
        return v.reshape(-1, P).T

    src = rows(a["src"], EPAD)
    dst = rows(a["dst"], EPAD, N_NODES)
    edge = rows(a["edge_attr_65"], EPAD)
    ones = np.ones((1, EPAD), edge.dtype)
    laid = {
        "x": rows(a["x"], NPAD),
        "src": by_tile(src), "dst": by_tile(dst), "dst_line": dst,
        "dst_next": by_tile(np.concatenate([dst[1:], np.full(1, NPAD, dst.dtype)])),
        "polarity": by_tile(edge[:, 0]),
        "edge_t": np.concatenate([edge[:, 1:].T, ones]),
        "w1r_t": a["W1r"].T, "w1l_t": a["W1l"].T, "w2r_t": a["W2r"].T, "w2l_t": a["W2l"].T,
        "wg1_t": a["W_g1"].T, "wg2_t": a["W_g2"].T, "wle_t": a["W_le"].T, "we2": a["W_e2"],
        "we1_t": a["W_e1"].T, "be1": a["b_e1"], "be2": column(a["b_e2"]),
        "b1": a["b1"], "b2": a["b2"], "bg1": a["b_g1"], "bg2": a["b_g2"], "ble": a["b_le"],
        "b1_col": column(a["b1"]), "ln_g": column(a["ln_g"]), "ln_b": column(a["ln_b"]),
    }
    nc = bacc.Bacc("TRN2", target_bir_lowering=False, num_devices=1)
    arrays, tensors = {}, {}
    for name, v in laid.items():
        v = np.ascontiguousarray(v)
        arrays["in_" + name] = v
        tensors[name] = nc.dram_tensor("in_" + name, v.shape, mybir.dt.from_np(v.dtype), kind="ExternalInput").ap()
    out = nc.dram_tensor("out_rows", (NPAD, D), F32, kind="ExternalOutput").ap()
    build_program(nc, tensors, out)
    result = run_bass_kernel_spmd(nc, [arrays], core_ids=[0])
    return result.results[0]["out_rows"][:N_NODES]
```
